# Optimizing a Trainium2 kernel written in Bass

```python
import numpy as np
import jax
import jax.numpy as jnp

def _softmax(x, axis=-1):
    return jax.nn.softmax(x, axis=axis)

def _gelu(x):
    return jax.nn.gelu(x, approximate=True)

def _silu(x):
    return jax.nn.silu(x)

def _sigmoid(x):
    return jax.nn.sigmoid(x)

def _layernorm(x, axis=-1, eps=1e-05):
    m = jnp.mean(x, axis=axis, keepdims=True)
    v = jnp.var(x, axis=axis, keepdims=True)
    return (x - m) / jnp.sqrt(v + eps)

def _scatter_add(tgt, idx, src, axis=0):
    return tgt.at[idx].add(src)

def _segment_sum(src, seg, n):
    return jax.ops.segment_sum(src, seg, n)
kernel_name = 'mk_vit_tower_d1_tok_img4096_r4_6351e1'

def setup_inputs(seed: int=0):
    np.random.seed(seed)
    _w = jnp.asarray

    def _rec_inputs():
        import jax
        import jax.numpy as jnp
        _rk = jax.random.key(seed)
        x = -0.00348982 + 0.707501 * jax.random.normal(jax.random.fold_in(_rk, 1), (32, 128, 64, 2), jnp.float32)
        return x
    x = _rec_inputs()

    def _L0_tok_setup():
        import jax, jax.numpy as jnp
        import numpy as np
        H, N, S, CH, LEN = (128, 64, 128, 1, 1024)

        def _s4d_kernel(log_dt, C, B, inv_A_real, A_imag, L):
            dt = jnp.exp(log_dt)
            Cc = C[..., 0] + 1j * C[..., 1]
            Bc = B[..., 0] + 1j * B[..., 1]
            A = -jnp.exp(inv_A_real) + 1j * A_imag
            rep = H // A.shape[0]
            A = jnp.tile(A, (rep, 1))
            Bc = jnp.tile(Bc, (rep, 1))
            dtA = A * dt[:, None]
            Cc = Bc[None, :, :] * Cc
            Cc = Cc * (jnp.exp(dtA) - 1.0) / A
            ell = jnp.arange(L, dtype=jnp.float32)
            V = jnp.exp(dtA[:, :, None] * ell)
            K = 2.0 * jnp.einsum('chn,hnl->chl', Cc, V).real
            return K.astype(jnp.float32)
        key = jax.random.key(seed)
        k1, k2 = jax.random.split(key, 2)
        log_dt = jax.random.uniform(k1, (H,), minval=float(np.log(0.001)), maxval=float(np.log(0.1))).astype(jnp.float32)
        inv_A_real = jnp.full((S, N), float(np.log(0.5)), dtype=jnp.float32)
        A_imag = jnp.tile((np.pi * jnp.arange(N, dtype=jnp.float32))[None, :], (S, 1))
        B = jnp.stack([jnp.ones((S, N), jnp.float32), jnp.zeros((S, N), jnp.float32)], axis=-1)
        C = (jax.random.normal(k2, (CH, H, N, 2)) * 0.5 ** 0.5).astype(jnp.float32)
        return {'log_dt': log_dt, 'C': C, 'B': B, 'inv_A_real': inv_A_real, 'A_imag': A_imag, 'L': LEN}
    _L0_tok_all = _L0_tok_setup()
    _L0_tok_in = {k: v for k, v in _L0_tok_all.items() if k in ('log_dt', 'B', 'inv_A_real', 'A_imag')}
    del _L0_tok_all

    def _L0_attn_setup():
        import jax, jax.numpy as jnp
        import numpy as np
        IN_FEATURES = 1024
        OUT_FEATURES = 1024
        WEIGHT_SPARSITY = 0.9
        key = jax.random.key(seed)
        kx, kw, km, kb = jax.random.split(key, 4)
        x = jax.random.normal(kx, (4, 512, IN_FEATURES), dtype=jnp.float32)
        dense_w = jax.random.normal(kw, (OUT_FEATURES, IN_FEATURES), dtype=jnp.float32)
        mask = jax.random.uniform(km, (OUT_FEATURES, IN_FEATURES)) >= WEIGHT_SPARSITY
        weight = dense_w * mask.astype(jnp.float32)
        bias = jax.random.uniform(kb, (OUT_FEATURES,), dtype=jnp.float32)
        return {'x': x, 'weight': weight, 'bias': bias}
    _L0_attn_all = _L0_attn_setup()
    _L0_attn_in = {k: v for k, v in _L0_attn_all.items() if k in ('weight', 'bias')}
    del _L0_attn_all

    def _L0_ffn_setup():
        import jax, jax.numpy as jnp
        import numpy as np
        SCALE = 16.0 / 8.0
        key = jax.random.key(seed)
        ks = jax.random.split(key, 6)
        B, S, IN, OUT, E, R = (4, 512, 1024, 1024, 4, 8)
        x = jax.random.normal(ks[0], (B, S, IN), dtype=jnp.float32)
        W = jax.random.normal(ks[1], (OUT, IN), dtype=jnp.float32) * 0.02
        b = jax.random.normal(ks[2], (OUT,), dtype=jnp.float32) * 0.02
        A = jax.random.normal(ks[3], (E, R, IN), dtype=jnp.float32) * 0.02
        Bm = jax.random.normal(ks[4], (E, OUT, R), dtype=jnp.float32) * 0.02
        Wr = jax.random.normal(ks[5], (E, IN), dtype=jnp.float32) * 0.02
        return {'x': x, 'W': W, 'b': b, 'A': A, 'Bm': Bm, 'Wr': Wr}
    _L0_ffn_all = _L0_ffn_setup()
    _L0_ffn_in = {k: v for k, v in _L0_ffn_all.items() if k in ('W', 'b', 'A', 'Bm', 'Wr')}
    del _L0_ffn_all
    return {'x': x, 'L0_tok_log_dt': _L0_tok_in['log_dt'], 'L0_tok_B': _L0_tok_in['B'], 'L0_tok_inv_A_real': _L0_tok_in['inv_A_real'], 'L0_tok_A_imag': _L0_tok_in['A_imag'], 'L0_attn_weight': _L0_attn_in['weight'], 'L0_attn_bias': _L0_attn_in['bias'], 'L0_ffn_W': _L0_ffn_in['W'], 'L0_ffn_b': _L0_ffn_in['b'], 'L0_ffn_A': _L0_ffn_in['A'], 'L0_ffn_Bm': _L0_ffn_in['Bm'], 'L0_ffn_Wr': _L0_ffn_in['Wr']}

def reference(x, L0_tok_log_dt, L0_tok_B, L0_tok_inv_A_real, L0_tok_A_imag, L0_attn_weight, L0_attn_bias, L0_ffn_W, L0_ffn_b, L0_ffn_A, L0_ffn_Bm, L0_ffn_Wr):
    import jax
    import jax.numpy as jnp

    def _L0_tok_ref(log_dt, C, B, inv_A_real, A_imag, L):
        import jax, jax.numpy as jnp
        import numpy as np
        H, N, S, CH, LEN = (128, 64, 128, 1, 1024)

        def _s4d_kernel(log_dt, C, B, inv_A_real, A_imag, L):
            dt = jnp.exp(log_dt)
            Cc = C[..., 0] + 1j * C[..., 1]
            Bc = B[..., 0] + 1j * B[..., 1]
            A = -jnp.exp(inv_A_real) + 1j * A_imag
            rep = H // A.shape[0]
            A = jnp.tile(A, (rep, 1))
            Bc = jnp.tile(Bc, (rep, 1))
            dtA = A * dt[:, None]
            Cc = Bc[None, :, :] * Cc
            Cc = Cc * (jnp.exp(dtA) - 1.0) / A
            ell = jnp.arange(L, dtype=jnp.float32)
            V = jnp.exp(dtA[:, :, None] * ell)
            K = 2.0 * jnp.einsum('chn,hnl->chl', Cc, V).real
            return K.astype(jnp.float32)
        return _s4d_kernel(log_dt, C, B, inv_A_real, A_imag, L)

    def _L0_attn_ref(x, weight, bias):
        import jax, jax.numpy as jnp
        import numpy as np
        IN_FEATURES = 1024
        OUT_FEATURES = 1024
        WEIGHT_SPARSITY = 0.9
        return jnp.einsum('bsi,oi->bso', x, weight) + bias

    def _L0_ffn_ref(x, W, b, A, Bm, Wr):
        import jax, jax.numpy as jnp
        import numpy as np
        SCALE = 16.0 / 8.0
        base_out = jnp.einsum('bsi,oi->bso', x, W) + b
        gates = jax.nn.softmax(jnp.einsum('bsi,ei->bse', x, Wr), axis=-1)
        proj_r = jnp.einsum('bsi,eri->bser', x, A)
        lora_out = jnp.einsum('bser,eor->bseo', proj_r, Bm)
        lora_mix = jnp.einsum('bse,bseo->bso', gates * SCALE, lora_out)
        return base_out + lora_mix
    h = _L0_tok_ref(L0_tok_log_dt, x, L0_tok_B, L0_tok_inv_A_real, L0_tok_A_imag, 1024)
    h = h + _L0_attn_ref(_layernorm(h, axis=-1), L0_attn_weight, L0_attn_bias)
    h = h + _L0_ffn_ref(_layernorm(h, axis=-1), L0_ffn_W, L0_ffn_b, L0_ffn_A, L0_ffn_Bm, L0_ffn_Wr)
    return h

_drawn_inputs = setup_inputs


def setup_inputs(seed=0):
    import zlib

    import numpy as np

    out = dict(_drawn_inputs(seed))
    spreads = {'L0_tok_inv_A_real': (-0.6931471824645996, 0.2)}
    factors = {'L0_ffn_b': 30.175, 'L0_ffn_A': 8.0, 'L0_ffn_Bm': 8.0, 'L0_ffn_Wr': 8.0}
    for name, (base, spread) in spreads.items():
        noise = np.random.default_rng([zlib.crc32(name.encode()), seed]).standard_normal(out[name].shape)
        drawn = base * np.exp(spread * noise) if base else spread * noise
        out[name] = jnp.asarray(drawn.astype(out[name].dtype))
    for name, factor in factors.items():
        out[name] = (out[name] * factor).astype(out[name].dtype)
    return out
```

```python
from contextlib import ExitStack
from math import factorial, log, pi

import concourse.bass as bass
from concourse import mybir

F32 = mybir.dt.float32
F32R = mybir.dt.float32r
F16 = mybir.dt.float16
U32 = mybir.dt.uint32
ALU = mybir.AluOpType
ACT = mybir.ActivationFunctionType
AX = mybir.AxisListType

P = 128
C, H, N = 32, 128, 64
L = 1024
E, R = 4, 8
ER = E * R
G = ER + E
KB = L // P
HT = 8
TT = HT * C
TILES = H // HT
SUB = TT // P
HS = P // C
KL = 3 * ER + 2
HALF = L // 2

XSCALE = 256.0
WSCALE = 2.0 ** 13
LORA_SCALE = 2.0
EPS = 1e-5
MAGIC = 1.5 * 2.0 ** 23
TWO_PI_HI = 6.28125
TWO_PI_LO = 2 * pi - TWO_PI_HI
LN2 = log(2)
LN2_HI = 0.693359375
LN2_LO = LN2 - LN2_HI
EXPS = 14
NOT_SIGN = 0x7FFFFFFF
EXPONENT = 0x7F800000
BELOW_PI = 3.1415925

SLOTS = 4
ATTN_BLOCKS = KB
BLOCKS = 2 * KB + 1


def at_least(engine, semaphore, value):
    if isinstance(value, int) and value <= 0:
        return
    engine.wait_ge(semaphore, value)


def program(nc, x, log_dt, B, inv_A_real, A_imag, attn_w, attn_b, ffn_w, ffn_b, lora_a, lora_b,
            gate_w, out):
    with ExitStack() as ctx:
        def sb(name, shape, dt=F32):
            return ctx.enter_context(nc.sbuf_tensor(name, shape, dt))

        def sem(name):
            return ctx.enter_context(nc.semaphore(name))

        wa_hi = sb("wa_hi", [P, KB, L], F16)
        wa_lo = sb("wa_lo", [P, KB, L], F16)
        wf_hi = sb("wf_hi", [P, KB, L], F16)
        wf_lo = sb("wf_lo", [P, KB, L], F16)
        wg_hi = sb("wg_hi", [P, KB, G], F16)
        wg_lo = sb("wg_lo", [P, KB, G], F16)
        lb = sb("lb", [KL, L], F32R)
        ident = sb("ident", [P, P])
        ident16 = sb("ident16", [P, P], F16)
        mean_w = sb("mean_w", [P, P])
        steps_b = sb("steps_b", [P, P])
        steps_a = sb("steps_a", [P, KB + 2])
        magic = sb("magic", [P, 1])
        sin_scale = sb("sin_scale", [P, 1])
        sin_bias = sb("sin_bias", [P, 1])
        half_pi = sb("half_pi", [P, 1])
        q1 = sb("q1", [P, KB, H])
        q2 = sb("q2", [P, KB, H])
        z_re = sb("z_re", [P, H])
        z_im = sb("z_im", [P, H])
        attn_unscale = sb("attn_unscale", [P, KB])
        attn_bias = sb("attn_bias", [P, KB])
        ffn_unscale = sb("ffn_unscale", [P, 1])
        x_raw = sb("x_raw", [P, SUB, 2, 2 * N])
        x_t = sb("x_t", [P, 2, TT])
        phase = sb("phase", [P, HT, P])
        decay = sb("decay", [P, HT, P])
        turn = sb("turn", [P, HT, P])
        u = sb("u", [P, HT, P])
        m = sb("m", [P, HT, KB, C])
        m_im = sb("m_im", [P, HT, KB, C])
        h = sb("h", [P, KB, TT])
        h2 = sb("h2", [P, KB, TT])
        h2_tok = sb("h2_tok", [P, SUB, L])
        d1 = sb("d1", [P, KB, TT])
        d2 = sb("d2", [P, KB, TT])
        squares = sb("squares", [P, KB, TT])
        x1_hi = sb("x1_hi", [P, KB, TT], F16)
        x1_lo = sb("x1_lo", [P, KB, TT], F16)
        x2_hi = sb("x2_hi", [P, KB, TT], F16)
        x2_lo = sb("x2_lo", [P, KB, TT], F16)
        attn_out = sb("attn_out", [P, 2, 2, TT])
        result = sb("result", [P, SUB, L])
        sum_1, sum_2 = sb("sum_1", [P, TT]), sb("sum_2", [P, TT])
        ssq_1, ssq_2 = sb("ssq_1", [P, TT]), sb("ssq_2", [P, TT])
        var_1, var_2 = sb("var_1", [P, TT]), sb("var_2", [P, TT])
        rstd_1, rstd_2 = sb("rstd_1", [P, TT]), sb("rstd_2", [P, TT])
        newton = sb("newton", [P, TT])
        mean_2 = sb("mean_2", [P, TT])
        gates = sb("gates", [P, SUB, E])
        gate_stat = sb("gate_stat", [P, SUB])
        lora = sb("lora", [P, SUB, ER])
        lora_split = sb("lora_split", [P, SUB, KL], F32R)
        lora_t = sb("lora_t", [KL, SUB, P], F32R)

        ps_attn = [ctx.enter_context(nc.psum_tensor(f"ps_attn{i}", [P, 2, TT], F32)) for i in range(2)]
        ps_ffn = [ctx.enter_context(nc.psum_tensor(f"ps_ffn{i}", [P, 2, HALF], F32)) for i in range(2)]
        ps_stat = ctx.enter_context(nc.psum_tensor("ps_stat", [P, HALF], F32))
        ps_gate = ctx.enter_context(nc.psum_tensor("ps_gate", [P, HALF], F32))

        s_const = sem("constants_ready")
        s_small = sem("small_inputs_loaded")
        s_pre_act = sem("prologue_act_done")
        s_pre_dve = sem("prologue_dve_done")
        s_pre_pe = sem("prologue_pe_done")
        s_wload = [sem(f"weight_block_loaded_{i}") for i in range(SLOTS)]
        s_whi = sem("weight_hi_done")
        s_wlo = [sem("weight_lo_done_by_dve"), sem("weight_lo_done_by_pool")]
        s_wscale = sem("weight_scale_done")
        s_wmax = sem("weight_max_done")
        s_wall = sem("weight_max_over_partitions")
        s_wturn = sem("weight_transposed")
        s_wcopy_hi = sem("weight_hi_copied")
        s_wcopy_lo = sem("weight_lo_copied")
        s_lb = sem("lora_b_loaded")
        s_lbn = sem("lora_b_split")
        s_wscaled = sem("weight_scaled")
        s_wg = sem("lora_a_loaded")
        s_power = sem("weight_power_done")
        s_fill = sem("fills_ready")
        s_x = sem("x_loaded")
        s_xt = sem("x_transposed")
        s_xt_sb = sem("x_transposed_copied")
        s_phase = sem("phase_ready")
        s_arg = sem("exponent_ready")
        s_turns = sem("turns_ready")
        s_decay = sem("decay_ready")
        s_reduce = sem("phase_reduced")
        s_sin = sem("sines_ready")
        s_u = sem("u_ready")
        s_terms = sem("m_terms_ready")
        s_m = sem("m_ready")
        s_s4 = sem("s4_product_done")
        s_h = sem("h_ready")
        s_sum1, s_sum2 = sem("sum1_ready"), sem("sum2_ready")
        s_mean1, s_mean2 = sem("mean1_done"), sem("mean2_done")
        s_mean2_sb = sem("mean2_copied")
        s_d1, s_d2 = sem("centred1_ready"), sem("centred2_ready")
        s_sq1, s_sq2 = sem("squares1_ready"), sem("squares2_ready")
        s_ssq1, s_ssq2 = sem("square_sum1_ready"), sem("square_sum2_ready")
        s_var1, s_var2 = sem("var1_done"), sem("var2_done")
        s_vv1, s_vv2 = sem("var1_copied"), sem("var2_copied")
        s_log1, s_log2 = sem("log_var1_ready"), sem("log_var2_ready")
        s_y1, s_y2 = sem("rstd_guess1_ready"), sem("rstd_guess2_ready")
        s_nw1, s_nw2 = sem("newton1_done"), sem("newton2_done")
        s_xn1, s_xn2 = sem("normalised1_ready"), sem("normalised2_ready")
        s_hi1, s_hi2 = sem("x1_hi_ready"), sem("x2_hi_ready")
        s_x1, s_x2 = sem("x1_ready"), sem("x2_ready")
        s_attn = sem("attn_product_done")
        s_attn_sb = sem("attn_product_copied")
        s_h2 = sem("h2_ready")
        s_h2t = sem("h2_transposed")
        s_h2_tok = sem("h2_by_token_ready")
        s_proj = sem("projections_done")
        s_soft = sem("softmax_step_done")
        s_gexp = sem("gate_exponentials_ready")
        s_lora_t = sem("lora_transposed")
        s_lora_sb = sem("lora_transposed_copied")
        s_ffn = sem("ffn_product_done")
        s_result = sem("result_ready")
        s_out = [sem("result_stored_0"), sem("result_stored_1")]

        x_rows = x.rearrange("(k c) h n r -> k c h (n r)", k=SUB)
        out_rows = out.rearrange("c h l -> h c l")
        attn_rows = attn_w.rearrange("(j p) i -> j p i", p=P)
        ffn_rows = ffn_w.rearrange("(j p) i -> j p i", p=P)

        slots = [b[:, i, :] for b in (result, h2_tok) for i in range(SUB)]
        chunk_hi = x2_hi[:, :, :].rearrange("p k t -> p (k t)").rearrange("p (s l) -> p s l", s=2)
        chunk_lo = x2_lo[:, :, :].rearrange("p k t -> p (k t)").rearrange("p (s l) -> p s l", s=2)
        NA = KB + 2
        area = {}
        flat = {"h2": h2[:, :, :].rearrange("p k t -> p (k t)"),
                "m": m[:, :, :, :].rearrange("p h a c -> p (h a c)"),
                "d2": d2[:, :, :].rearrange("p k t -> p (k t)"),
                "sq": squares[:, :, :].rearrange("p k t -> p (k t)"),
                "d1": d1[:, :, :].rearrange("p k t -> p (k t)")}
        used = dict.fromkeys(flat, 0)

        def scratch(name, where, *shape):
            n = 1
            for k in shape:
                n *= k
            a = flat[where][:, used[where]:used[where] + n]
            used[where] += n
            assert used[where] <= KB * TT
            area[name] = a if len(shape) == 1 else a.rearrange("p (a b) -> p a b", b=shape[-1])
            return area[name]

        ldt, ia, ai, bb = (scratch("ldt", "h2", 1), scratch("ia", "h2", N), scratch("ai", "h2", N),
                           scratch("bb", "h2", N, 2))
        dt, ea = scratch("dt", "h2", 1), scratch("ea", "h2", N)
        exp_in, exp_out = flat["h2"][:, 0:1 + N], flat["h2"][:, 1 + 4 * N:2 + 5 * N]
        exp_k = scratch("exp_k", "h2", 1 + N)
        zr, zi = scratch("zr", "h2", 2, N), scratch("zi", "h2", 2, N)
        th, ex, em = scratch("th", "h2", N), scratch("ex", "h2", N), scratch("em", "h2", N)
        cm, e_re, e_im = scratch("cm", "h2", N), scratch("e_re", "h2", N), scratch("e_im", "h2", N)
        den, t_re, t_im = scratch("den", "h2", N), scratch("t_re", "h2", N), scratch("t_im", "h2", N)
        g_re, g_im, tmp = scratch("g_re", "h2", N), scratch("g_im", "h2", N), scratch("tmp", "h2", N)
        tmp2 = scratch("tmp2", "h2", N)
        ph, kk, ph_abs = scratch("ph", "m", NA, N), scratch("kk", "m", NA, N), scratch("pa", "m", NA, N)
        sn, cs = scratch("sn", "d2", NA, N), scratch("cs", "d2", NA, N)
        wexp = scratch("wexp", "d2", KB, N)
        w_re, w_im = scratch("w_re", "sq", KB, N), scratch("w_im", "sq", KB, N)
        qa, qb = scratch("qa", "sq", KB, N), scratch("qb", "sq", KB, N)
        q1n, q2n = scratch("q1n", "d1", KB, 2 * N), scratch("q2n", "d1", KB, 2 * N)
        wg_rows = attn_out[:, :, :, :].rearrange("p a b t -> p (a b t)")[0:G, :]
        w_max = sb("w_max", [P, KB])
        f_max = sb("f_max", [P, KB + 1])
        f_top = sb("f_top", [P, 2])
        f_pow = sb("f_pow", [P, 1])
        ffn_scale = sb("ffn_scale", [P, 1])
        w_scale = sb("w_scale", [P, KB])
        w_pow = sb("w_pow", [P, KB])
        lbn = flat["d2"][:, 0:KB * KL].bitcast(F32R).rearrange("p (a b) -> p a b", b=KL)
        lbm, lbb = scratch("lbm", "d2", KB, ER), scratch("lbb", "h2", KB)

        def m_term(T, part):
            c = x_t[:, part, :].rearrange("p (c h) -> p h c", h=HT).unsqueeze(2)\
                .broadcast_to((P, HT, KB, C))
            f = (q1, q2)[part][:, :, bass.ds(T * HT, HT)].rearrange("p a h -> p h a").unsqueeze(3)\
                .broadcast_to((P, HT, KB, C))
            return c, f, (m, m_im)[part][:, :, :, :]

        def x2_of(t):
            return (x1_hi, x1_lo) if isinstance(t, int) and t == TILES - 1 else (x2_hi, x2_lo)

        def acc_of(t, i):
            if isinstance(t, int) and t == TILES - 1:
                return [ps[:, :, :].rearrange("p a b -> p (a b)") for ps in ps_attn] if i == 0 else \
                    [ps_ffn[0][:, o, :] for o in range(2)]
            return [ps_ffn[i][:, o, :] for o in range(2)]

        def load_of(n):
            return n if n < ATTN_BLOCKS else n + KB - 1

        def arrived(engine, load):
            engine.wait_ge(s_wload[load % SLOTS], 16 * (load // SLOTS + 1))

        def rows_of(n):
            if n < ATTN_BLOCKS:
                return P, slots[load_of(n) % SLOTS], w_scale[:, n:n + 1]
            if n == ATTN_BLOCKS:
                return G, wg_rows, ffn_scale[0:G, :]
            return P, slots[load_of(n) % SLOTS], ffn_scale[:, :]

        def split_of(n):
            rows = rows_of(n)[0]
            return chunk_hi[0:rows, n % 2, :], chunk_lo[0:rows, n % 2, :]

        def lo_done(engine, n):
            if n < ATTN_BLOCKS:
                engine.wait_ge(s_wlo[n % 2], n // 2 + 1)
            else:
                engine.wait_ge(s_wlo[0], n + 1 - ATTN_BLOCKS // 2)

        def turned_banks(n):
            if n < ATTN_BLOCKS:
                return [ps_attn[part][:, :, :].rearrange("p a b -> p (a b)").bitcast(F16) for part in range(2)]
            return [ps_ffn[n % 2][:, part, :].bitcast(F16) for part in range(2)]

        def turned(n, part):
            rows = rows_of(n)[0]
            return turned_banks(n)[part].rearrange("p (k o) -> p k o", k=KB)[:, :, 0:rows]

        def weights_of(n, part):
            if n < ATTN_BLOCKS:
                return (wa_hi, wa_lo)[part][:, :, n * P:(n + 1) * P]
            if n == ATTN_BLOCKS:
                return (wg_hi, wg_lo)[part][:, :, :]
            return (wf_hi, wf_lo)[part][:, :, (n - KB - 1) * P:(n - KB) * P]

        block = ctx.enter_context(nc.Block())

        @block.sync
        def _(sp):
            for dst, src in ((ldt, log_dt.rearrange("(h a) -> h a", a=1)), (ia, inv_A_real), (ai, A_imag),
                             (bb, B)):
                sp.dma_start(dst, src).then_inc(s_small, 16)

            def load_x(T):
                at_least(sp, s_xt, T)
                for k in range(SUB):
                    for twice in range(2):
                        sp.dma_start(x_raw[:, k, twice, :], x_rows[k, :, bass.ds(T * HT, HT), :])\
                            .then_inc(s_x, 16)

            load_x(0)
            sp.dma_start(attn_bias[:, :], attn_b.rearrange("(j p) -> p j", p=P),
                         allow_slow_non_contiguous=True).then_inc(s_small, 16)

            def load_blocks(first, end):
                for n in range(first, end):
                    last = n - SLOTS
                    if last >= 2 * KB:
                        lo_done(sp, last - KB + 1)
                    elif last >= KB:
                        sp.wait_ge(s_wmax, last + 2)
                    elif last >= 0:
                        lo_done(sp, last)
                    src = attn_rows[n] if n < KB else ffn_rows[n % KB]
                    sp.dma_start(slots[n % SLOTS], src).then_inc(s_wload[n % SLOTS], 16)

            load_blocks(0, KB)
            sp.dma_start(wg_rows[0:ER, :], lora_a.rearrange("e r i -> (e r) i")).then_inc(s_wg, 16)
            sp.dma_start(wg_rows[ER:G, :], gate_w).then_inc(s_wg, 16)
            load_blocks(KB, KB + 2)
            load_x(1)
            load_blocks(KB + 2, 2 * KB)
            sp.wait_ge(s_pre_dve, EXPS + 41)
            for j in range(KB):
                sp.dma_start(lbm[:, j, :].rearrange("p (e r) -> p e r", e=E),
                             lora_b[:, j * P:(j + 1) * P, :].rearrange("e p r -> p e r")).then_inc(s_lb, 16)
            sp.dma_start(lbb, ffn_b.rearrange("(j p) -> p j", p=P),
                         allow_slow_non_contiguous=True).then_inc(s_lb, 16)
            load_blocks(2 * KB, 3 * KB)

            def store(t, i):
                sp.wait_ge(s_result, 2 * t + i + 1)
                sp.dma_start(out_rows[bass.ds(t * HT + i * HS, HS), :, :], result[:, i, :])\
                    .then_inc(s_out[i], 16)

            load_x(2)
            load_x(3)
            for i in range(SUB):
                store(0, i)
            with sp.Fori(2, TILES - 2) as t:
                load_x(t + 2)
                for i in range(SUB):
                    store(t - 1, i)
            for t in (TILES - 3, TILES - 2, TILES - 1):
                for i in range(SUB):
                    store(t, i)
            for i in range(SUB):
                sp.wait_ge(s_out[i], 16 * TILES)

        @block.tensor
        def _(pe):
            def turn_x(T, last_reader, count):
                pe.wait_ge(s_x, 64 * T + 64)
                at_least(pe, last_reader, count)
                for part in range(2):
                    for k in range(SUB):
                        rows = x_raw[:, k, :, :].rearrange("p d (n r) -> p r (d n)", r=2)[:, part, :]
                        mm = pe.transpose(ps_stat[:, part * TT + k * P:part * TT + (k + 1) * P], rows,
                                          ident[:, :])
                mm.then_inc(s_xt, 1)

            def s4(T, last_reader, count):
                pe.wait_ge(s_u, T + 1)
                pe.wait_ge(s_m, T + 1)
                at_least(pe, last_reader, count)
                for q in range(HT // 2):
                    for e in range(2):
                        mm = pe.matmul(ps_ffn[q // 2][:, q % 2, e * TT:(e + 1) * TT], u[:, 2 * q + e, :],
                                       m[:, 2 * q + e, :, :].rearrange("p a c -> p (a c)"),
                                       start=True, stop=True)
                    mm.then_inc(s_s4, 1)

            def stat(T, ready, sums, reader, count, done):
                pe.wait_ge(ready, T + 1)
                at_least(pe, reader, count)
                pe.matmul(ps_stat[:, 0:TT], mean_w[:, :], sums[:, :], start=True, stop=True).then_inc(done, 1)

            def attn_pair(t, j2):
                at_least(pe, s_attn_sb, 4 * t + j2 - 1)
                for e in range(2):
                    cols = slice((2 * j2 + e) * P, (2 * j2 + e + 1) * P)
                    o = ps_attn[j2 % 2][:, e, :]
                    for k in range(KB):
                        pe.matmul(o, wa_hi[:, k, cols], x1_hi[:, k, :], start=k == 0, stop=False)
                        pe.matmul(o, wa_hi[:, k, cols], x1_lo[:, k, :], start=False, stop=False)
                        mm = pe.matmul(o, wa_lo[:, k, cols], x1_hi[:, k, :], start=False, stop=k == KB - 1)
                mm.then_inc(s_attn, 1)

            def turn_h2(t, i):
                pe.wait_ge(s_h2, 4 * t + 4)
                at_least(pe, s_result, 2 * t + i - 1)
                for k in range(KB):
                    mm = pe.transpose(ps_ffn[i][:, k // 4, (k % 4) * P:(k % 4 + 1) * P],
                                      h2[:, k, i * P:(i + 1) * P], ident[:, :])
                mm.then_inc(s_h2t, 1)

            def project(t):
                pe.wait_ge(s_x2, t + 1)
                at_least(pe, s_lora_sb, t)
                x2_hi, x2_lo = x2_of(t)
                for i in range(SUB):
                    o = ps_gate[:, i * G:(i + 1) * G]
                    tok = slice(i * P, (i + 1) * P)
                    for k in range(KB):
                        pe.matmul(o, x2_hi[:, k, tok], wg_hi[:, k, :], start=k == 0, stop=False)
                        pe.matmul(o, x2_hi[:, k, tok], wg_lo[:, k, :], start=False, stop=False)
                        mm = pe.matmul(o, x2_lo[:, k, tok], wg_hi[:, k, :], start=False, stop=k == KB - 1)
                mm.then_inc(s_proj, 1)

            def turn_lora(t):
                pe.wait_ge(s_soft, 9 * t + 9)
                for i in range(SUB):
                    mm = pe.transpose(ps_gate[0:KL, P + i * P:P + (i + 1) * P],
                                      lora_split[:, i, :].bitcast(F32), ident[:, :])
                mm.then_inc(s_lora_t, 1)

            def ffn_part(t, i, ks):
                tok = slice(i * P, (i + 1) * P)
                x2_hi, x2_lo = x2_of(t)
                acc = acc_of(t, i)
                for k in ks:
                    for xs, ws in ((x2_hi, wf_hi), (x2_hi, wf_lo), (x2_lo, wf_hi)):
                        for o in range(2):
                            pe.matmul(acc[o], xs[:, k, tok], ws[:, k, o * HALF:(o + 1) * HALF],
                                      start=k == 0 and xs is x2_hi and ws is wf_hi, stop=False)

            def ffn_end(t, i):
                pe.wait_ge(s_lora_sb, t + 1)
                for o in range(2):
                    mm = pe.matmul(acc_of(t, i)[o], lora_t[:, i, :], lb[:, o * HALF:(o + 1) * HALF],
                                   start=False, stop=True)
                mm.then_inc(s_ffn, 1)

            def ffn(t, free, counts, after_part, after_first, after_second):
                project(t)
                pe.wait_ge(free, counts[0])
                ffn_part(t, 0, range(0, 2))
                after_part()
                ffn_part(t, 0, range(2, KB - 1))
                turn_lora(t)
                ffn_part(t, 0, range(KB - 1, KB))
                ffn_end(t, 0)
                after_first()
                pe.wait_ge(free, counts[1])
                ffn_part(t, 1, range(0, 3))
                after_second()
                ffn_part(t, 1, range(3, KB))
                ffn_end(t, 1)

            def nothing():
                pass

            def turn_weights(first, end):
                for n in range(first, end):
                    free = n if n < ATTN_BLOCKS else max(n - 1, ATTN_BLOCKS)
                    for part, (ready, copied) in enumerate(((lambda: pe.wait_ge(s_whi, n + 1), s_wcopy_hi),
                                                            (lambda: lo_done(pe, n), s_wcopy_lo))):
                        ready()
                        at_least(pe, copied, free)
                        rows, src, bank = rows_of(n)[0], split_of(n)[part], turned_banks(n)[part]
                        for k in range(KB):
                            mm = pe.transpose(bank[:, k * P:k * P + rows], src[:, k * P:(k + 1) * P],
                                              ident16[0:rows, 0:rows])
                        mm.then_inc(s_wturn, 1)

            def weights_copied(count):
                pe.wait_ge(s_wcopy_hi, count)
                pe.wait_ge(s_wcopy_lo, count)

            pe.wait_ge(s_const, 4)
            pe.wait_ge(s_fill, 1)
            pe.wait_ge(s_pre_dve, EXPS + 4)
            pe.transpose(ps_gate[:, 0:P], zr.rearrange("p a b -> p (a b)"), ident[:, :])
            pe.transpose(ps_gate[:, P:2 * P], zi.rearrange("p a b -> p (a b)"), ident[:, :]).then_inc(s_pre_pe, 1)
            turn_weights(0, 2)
            pe.wait_ge(s_pre_dve, EXPS + 41)
            for q, (src, dst) in enumerate(((q1n, ps_ffn[0]), (q2n, ps_ffn[1]))):
                for a in range(KB):
                    mm = pe.transpose(dst[:, a // 4, (a % 4) * P:(a % 4 + 1) * P], src[:, a, :], ident[:, :])
                mm.then_inc(s_pre_pe, 1)
            turn_x(0, s_const, 0)
            turn_weights(2, 3)
            s4(0, s_pre_act, 9)
            turn_weights(3, 4)
            stat(0, s_sum1, sum_1, s_xt_sb, 1, s_mean1)
            turn_weights(4, 6)
            stat(0, s_ssq1, ssq_1, s_d1, 1, s_var1)
            turn_weights(6, 8)

            def step_0():
                turn_x(1, s_vv1, 1)
                pe.wait_ge(s_x1, 1)
                weights_copied(ATTN_BLOCKS)
                attn_pair(0, 0)
                attn_pair(0, 1)
                turn_weights(8, 10)
                attn_pair(0, 2)
                turn_weights(10, 12)
                attn_pair(0, 3)
                weights_copied(12)
                s4(1, s_const, 0)
                pe.wait_ge(s_h, 8)
                turn_weights(12, 13)
                stat(1, s_sum1, sum_1, s_xt_sb, 2, s_mean1)
                turn_weights(13, 15)
                stat(1, s_ssq1, ssq_1, s_d1, 2, s_var1)
                turn_weights(15, 17)
                weights_copied(16)
                pe.wait_ge(s_lbn, 3)
                for j in range(KB):
                    mm = pe.transpose(ps_ffn[1][0:KL, j // 4, (j % 4) * P:(j % 4 + 1) * P],
                                      lbn[:, j, :].bitcast(F32), ident[:, :])
                mm.then_inc(s_pre_pe, 1)
                stat(0, s_sum2, sum_2, s_vv1, 2, s_mean2)

            def step(t):
                turn_x(t + 1, s_mean2_sb, t)
                turn_h2(t - 1, 0)
                pe.wait_ge(s_x1, t + 1)
                attn_pair(t, 0)
                turn_h2(t - 1, 1)
                attn_pair(t, 1)
                stat(t - 1, s_ssq2, ssq_2, s_xt_sb, t + 2, s_var2)
                attn_pair(t, 2)
                attn_pair(t, 3)
                s4(t + 1, s_h2_tok, 2 * t)
                ffn(t - 1, s_h, (4 * t + 6, 4 * t + 8),
                    lambda: stat(t + 1, s_sum1, sum_1, s_vv2, t, s_mean1),
                    lambda: stat(t + 1, s_ssq1, ssq_1, s_d1, t + 2, s_var1),
                    lambda: stat(t, s_sum2, sum_2, s_vv1, t + 2, s_mean2))

            step_0()
            weights_copied(BLOCKS)
            pe.wait_ge(s_pre_act, 10)
            step(1)
            with pe.Fori(2, TILES - 1) as t:
                step(t)
            t = TILES - 1
            turn_h2(t - 1, 0)
            pe.wait_ge(s_x1, t + 1)
            attn_pair(t, 0)
            turn_h2(t - 1, 1)
            attn_pair(t, 1)
            stat(t - 1, s_ssq2, ssq_2, s_mean2_sb, t, s_var2)
            attn_pair(t, 2)
            attn_pair(t, 3)

            def between():
                turn_h2(t, 0)
                stat(t, s_ssq2, ssq_2, s_mean2_sb, t + 1, s_var2)

            ffn(t - 1, s_h2_tok, (2 * t - 1, 2 * t),
                lambda: stat(t, s_sum2, sum_2, s_vv2, t, s_mean2), nothing, between)
            project(t)
            pe.wait_ge(s_attn_sb, 4 * TILES)
            ffn_part(t, 0, range(0, 4))
            turn_h2(t, 1)
            turn_lora(t)
            ffn_part(t, 0, range(4, KB))
            ffn_end(t, 0)
            pe.wait_ge(s_h2_tok, 2 * t + 1)
            ffn_part(t, 1, range(0, KB))
            ffn_end(t, 1)

        @block.scalar
        def _(act):
            def copy_x(T):
                act.wait_ge(s_xt, T + 1)
                at_least(act, s_terms, 2 * T)
                act.activation(x_t[:, :, :].rearrange("p a b -> p (a b)"), ps_stat[:, :], ACT.Copy)\
                    .then_inc(s_xt_sb, 1)

            def turns(T):
                act.wait_ge(s_phase, T + 1)
                at_least(act, s_u, T)
                act.activation(turn[:, :, :], phase[:, :, :], ACT.Identity, bias=magic[:, :],
                               scale=1 / (2 * pi)).then_inc(s_turns, 1)

            def decays(T):
                act.wait_ge(s_arg, T + 1)
                act.activation(decay[:, :, :], decay[:, :, :], ACT.Exp).then_inc(s_decay, 1)

            def sines(T):
                act.wait_ge(s_reduce, 5 * T + 5)
                act.activation(turn[:, :, :], phase[:, :, :], ACT.Sin, bias=sin_bias[:, :],
                               scale=sin_scale[:, :]).then_inc(s_sin, 1)

            def copy_h(T):
                at_least(act, s_h2, 4 * T)
                for q in range(HT // 2):
                    act.wait_ge(s_s4, 4 * T + q + 1)
                    act.activation(h[:, :, 2 * q * C:2 * (q + 1) * C].rearrange("p a (e c) -> p e a c", e=2),
                                   ps_ffn[q // 2][:, q % 2, :].rearrange("p (e a c) -> p e a c", e=2, a=KB),
                                   ACT.Copy).then_inc(s_h, 1)

            def square(T, d, ready, reader, count, done):
                act.wait_ge(ready, T + 1)
                at_least(act, reader, count)
                act.activation(squares[:, :, :], d[:, :, :], ACT.Square).then_inc(done, 1)

            def rstd_guess(T, var, rstd, ready, xn, log, done):
                act.wait_ge(ready, T + 1)
                at_least(act, xn, T)
                act.activation(rstd[:, :], var[:, :], ACT.Ln).then_inc(log, 1)
                act.wait_ge(log, T + 1)
                act.activation(rstd[:, :], rstd[:, :], ACT.Exp, scale=-0.5).then_inc(done, 1)

            def high_part(T, d, hi, ready, product, count, done):
                act.wait_ge(ready, T + 1)
                at_least(act, product, count)
                act.activation(hi[:, :, :], d[:, :, :], ACT.Copy).then_inc(done, 1)

            def copy_attn(t, j2):
                act.wait_ge(s_attn, 4 * t + j2 + 1)
                at_least(act, s_h2, 4 * t + j2 - 1)
                for e in range(2):
                    j = 2 * j2 + e
                    a = act.activation(attn_out[:, j2 % 2, e, :], ps_attn[j2 % 2][:, e, :], ACT.Identity,
                                       bias=attn_bias[:, j:j + 1], scale=attn_unscale[:, j:j + 1])
                a.then_inc(s_attn_sb, 1)

            def copy_h2(t, i):
                act.wait_ge(s_h2t, 2 * t + i + 1)
                at_least(act, s_result, 2 * t + i - 1)
                act.activation(h2_tok[:, i, :], ps_ffn[i][:, :, :].rearrange("p a b -> p (a b)"), ACT.Copy)\
                    .then_inc(s_h2_tok, 1)

            def gate_exp(t):
                act.wait_ge(s_soft, 9 * t + 2)
                g = gates[:, :, :].rearrange("p a b -> p (a b)")
                act.activation(g, g, ACT.Exp, scale=ffn_unscale[:, :]).then_inc(s_gexp, 1)

            def copy_mean2(t):
                act.wait_ge(s_mean2, t + 1)
                at_least(act, s_d2, t)
                act.activation(mean_2[:, :], ps_stat[:, 0:TT], ACT.Copy).then_inc(s_mean2_sb, 1)

            def weight_hi(n):
                rows, src, scale = rows_of(n)
                if n == ATTN_BLOCKS:
                    act.wait_ge(s_wg, 32)
                else:
                    arrived(act, load_of(n))
                act.wait_ge(s_wscale, 2 * min(n, KB) + 2)
                at_least(act, s_wturn, 2 * (n - 1))
                act.activation(split_of(n)[0], src, ACT.Copy, scale=scale).then_inc(s_whi, 1)

            def copy_weight(n, part):
                act.wait_ge(s_wturn, 2 * n + part + 1)
                act.activation(weights_of(n, part), turned(n, part), ACT.Copy)\
                    .then_inc((s_wcopy_hi, s_wcopy_lo)[part], 1)

            def copy_both(n):
                copy_weight(n, 0)
                copy_weight(n, 1)

            act.wait_ge(s_small, 80)
            act.wait_ge(s_fill, 1)
            act.wait_ge(s_pre_dve, EXPS + 4)
            act.activation(th, zr[:, 0, :], ACT.Tanh, scale=0.5).then_inc(s_pre_act, 1)
            act.activation(ex, zr[:, 0, :], ACT.Exp).then_inc(s_pre_act, 1)
            act.wait_ge(s_pre_dve, EXPS + 6)
            act.activation(wexp, wexp, ACT.Exp).then_inc(s_pre_act, 1)
            act.activation(kk, ph, ACT.Identity, bias=magic[:, :], scale=1 / (2 * pi)).then_inc(s_pre_act, 1)
            weight_hi(0)
            act.wait_ge(s_pre_dve, EXPS + 11)
            act.activation(sn, ph, ACT.Sin).then_inc(s_pre_act, 1)
            act.activation(cs, ph_abs, ACT.Sin, bias=half_pi[:, :], scale=-1.0).then_inc(s_pre_act, 1)

            act.wait_ge(s_pre_pe, 1)
            act.activation(z_re[:, :], ps_gate[:, 0:P], ACT.Copy)
            act.activation(z_im[:, :], ps_gate[:, P:2 * P], ACT.Copy).then_inc(s_pre_act, 1)
            weight_hi(1)
            copy_both(0)
            turns(0)
            copy_both(1)
            decays(0)
            act.wait_ge(s_pre_pe, 2)
            act.activation(q1[:, :, :].rearrange("p a b -> p (a b)"),
                           ps_ffn[0][:, :, :].rearrange("p a b -> p (a b)"), ACT.Copy).then_inc(s_pre_act, 1)
            act.wait_ge(s_pre_pe, 3)
            act.activation(q2[:, :, :].rearrange("p a b -> p (a b)"),
                           ps_ffn[1][:, :, :].rearrange("p a b -> p (a b)"), ACT.Copy).then_inc(s_pre_act, 1)
            copy_x(0)
            sines(0)
            weight_hi(2)
            weight_hi(3)
            copy_both(2)
            weight_hi(4)
            copy_h(0)
            copy_both(3)
            weight_hi(5)
            copy_both(4)
            square(0, d1, s_d1, s_const, 0, s_sq1)
            weight_hi(6)
            copy_both(5)
            weight_hi(7)
            rstd_guess(0, var_1, rstd_1, s_vv1, s_xn1, s_log1, s_y1)
            copy_both(6)
            high_part(0, d1, x1_hi, s_xn1, s_attn, 0, s_hi1)
            copy_both(7)

            def step_0():
                copy_x(1)
                turns(1)
                decays(1)
                weight_hi(8)
                weight_hi(9)
                act.wait_ge(s_whi, ATTN_BLOCKS + 1)
                lo_done(act, ATTN_BLOCKS)
                copy_attn(0, 0)
                copy_attn(0, 1)
                copy_weight(8, 0)
                weight_hi(10)
                copy_weight(9, 0)
                sines(1)
                weight_hi(11)
                copy_attn(0, 2)
                copy_weight(10, 0)
                weight_hi(12)
                copy_weight(11, 0)
                copy_attn(0, 3)
                weight_hi(13)
                copy_h(1)
                copy_weight(12, 0)
                weight_hi(14)
                square(1, d1, s_d1, s_const, 0, s_sq1)
                copy_weight(13, 0)
                weight_hi(15)
                copy_weight(14, 0)
                rstd_guess(1, var_1, rstd_1, s_vv1, s_xn1, s_log1, s_y1)
                weight_hi(16)
                copy_weight(15, 0)
                high_part(1, d1, x1_hi, s_xn1, s_attn, 4, s_hi1)
                copy_weight(16, 0)
                act.wait_ge(s_pre_pe, 4)
                act.activation(lb[:, :], ps_ffn[1][0:KL, :, :].rearrange("p a b -> p (a b)"), ACT.Copy)\
                    .then_inc(s_pre_act, 1)
                copy_mean2(0)
                square(0, d2, s_d2, s_ssq1, 2, s_sq2)

            def step(t):
                copy_x(t + 1)
                copy_h2(t - 1, 0)
                turns(t + 1)
                decays(t + 1)
                copy_attn(t, 0)
                copy_h2(t - 1, 1)
                sines(t + 1)
                copy_attn(t, 1)
                rstd_guess(t - 1, var_2, rstd_2, s_vv2, s_xn2, s_log2, s_y2)
                copy_attn(t, 2)
                high_part(t - 1, d2, x2_hi, s_xn2, s_ffn, 2 * (t - 1), s_hi2)
                copy_attn(t, 3)
                copy_h(t + 1)
                gate_exp(t - 1)
                square(t + 1, d1, s_d1, s_ssq2, t, s_sq1)
                rstd_guess(t + 1, var_1, rstd_1, s_vv1, s_xn1, s_log1, s_y1)
                high_part(t + 1, d1, x1_hi, s_xn1, s_attn, 4 * (t + 1), s_hi1)
                copy_mean2(t)
                square(t, d2, s_d2, s_ssq1, t + 2, s_sq2)

            step_0()
            step(1)
            with act.Fori(2, TILES - 1) as t:
                step(t)
            t = TILES - 1
            copy_h2(t - 1, 0)
            copy_attn(t, 0)
            copy_h2(t - 1, 1)
            copy_attn(t, 1)
            rstd_guess(t - 1, var_2, rstd_2, s_vv2, s_xn2, s_log2, s_y2)
            copy_attn(t, 2)
            high_part(t - 1, d2, x2_hi, s_xn2, s_ffn, 2 * (t - 1), s_hi2)
            copy_attn(t, 3)
            gate_exp(t - 1)
            copy_mean2(t)
            square(t, d2, s_d2, s_ssq1, TILES, s_sq2)
            copy_h2(t, 0)
            rstd_guess(t, var_2, rstd_2, s_vv2, s_xn2, s_log2, s_y2)
            high_part(t, d2, x2_of(t)[0], s_xn2, s_attn, 4 * TILES, s_hi2)
            gate_exp(t)
            copy_h2(t, 1)

        @block.gpsimd
        def _(pool):
            pool.memset(ident[:, :], 0.0).then_inc(s_wall, 1)
            pool.wait_ge(s_wall, 1)
            pool.affine_select(out=ident[:, :], in_=ident[:, :], compare_op=ALU.not_equal, fill=1.0, base=0,
                               pattern=[[-1, P]], channel_multiplier=1).then_inc(s_const, 1)
            pool.wait_ge(s_const, 1)
            pool.tensor_copy(ident16[:, :], ident[:, :]).then_inc(s_const, 1)
            pool.iota(steps_b[:, :], pattern=[[1, P]], base=0, channel_multiplier=0,
                      allow_small_or_imprecise_dtypes=True).then_inc(s_const, 1)
            pool.iota(steps_a[:, 2:NA], pattern=[[P, KB]], base=0, channel_multiplier=0,
                      allow_small_or_imprecise_dtypes=True).then_inc(s_const, 1)

            def wave(dst, z, T):
                return pool.tensor_tensor(dst[:, :, :],
                                          z[:, bass.ds(T * HT, HT)].unsqueeze(2).broadcast_to((P, HT, P)),
                                          steps_b[:, :].unsqueeze(1).broadcast_to((P, HT, P)), ALU.mult)

            def waves(T):
                at_least(pool, s_sin, T)
                wave(phase, z_im, T).then_inc(s_phase, 1)
                at_least(pool, s_u, T)
                wave(decay, z_re, T).then_inc(s_arg, 1)

            def m_terms(T, parts=(0, 1)):
                pool.wait_ge(s_xt_sb, T + 1)
                at_least(pool, s_s4, 4 * T)
                at_least(pool, s_m, T)
                for part in parts:
                    c, f, dst = m_term(T, part)
                    pool.tensor_tensor(dst, c, f, ALU.mult).then_inc(s_terms, 1)

            def weight_lo(n):
                rows, src, scale = rows_of(n)
                hi, lo = split_of(n)
                pool.wait_ge(s_whi, n + 1)
                pool.tensor_scalar(src, src, scale, None, ALU.mult).then_inc(s_wscaled, 1)
                pool.wait_ge(s_wscaled, n // 2 + 1)
                pool.tensor_tensor(lo, src, hi, ALU.subtract).then_inc(s_wlo[1], 1)

            def centre2(t):
                pool.wait_ge(s_mean2_sb, t + 1)
                at_least(pool, s_x2, t)
                pool.tensor_tensor(d2[:, :, :], h2[:, :, :],
                                   mean_2[:, :].unsqueeze(1).broadcast_to((P, KB, TT)), ALU.subtract)\
                    .then_inc(s_d2, 1)

            pool.wait_ge(s_pre_act, 7)
            waves(0)
            weight_lo(1)
            pool.wait_ge(s_pre_act, 9)
            m_terms(0, parts=(1,))
            weight_lo(3)
            weight_lo(5)
            weight_lo(7)
            waves(1)
            m_terms(1)
            pool.wait_ge(s_wmax, 2 * KB + 2)
            pool.partition_all_reduce(f_top[:, 1:2], f_top[:, 0:1], P, bass.bass_isa.ReduceOp.max)\
                .then_inc(s_wall, 1)
            centre2(0)
            waves(2)

            def step(t):
                m_terms(t + 1)
                centre2(t)
                waves(t + 2)

            step(1)
            with pool.Fori(2, TILES - 2) as t:
                step(t)
            m_terms(TILES - 1)
            centre2(TILES - 2)
            centre2(TILES - 1)

        @block.vector
        def _(dve):
            done = [0]

            def link(op, *args, **kwargs):
                at_least(dve, s_pre_dve, done[0])
                done[0] += 1
                op(*args, **kwargs).then_inc(s_pre_dve, 1)

            def tt(o, a, b, op):
                link(dve.tensor_tensor, o, a, b, op)

            for tile, value in ((mean_w[:, :], 1.0 / L), (magic[:, :], MAGIC), (half_pi[:, :], pi / 2),
                                (sin_scale[0:N, :], -1.0), (sin_scale[N:P, :], 1.0),
                                (sin_bias[0:N, :], pi / 2), (sin_bias[N:P, :], 0.0),
                                (steps_a[:, 0:1], 0.5), (steps_a[:, 1:2], 1.0), (f_max[:, :], 0.0)):
                last = dve.memset(tile, value)
            last.then_inc(s_fill, 1)
            dve.wait_ge(s_fill, 1)
            dve.wait_ge(s_const, 4)

            def split_scales(top, power, scale, unscale, n):
                dve.tensor_scalar(power, top, 1e-30, None, ALU.max).then_inc(s_power, 1)
                dve.wait_ge(s_power, 3 * n + 1)
                dve.tensor_scalar(power.bitcast(U32), power.bitcast(U32), EXPONENT, None, ALU.bitwise_and)\
                    .then_inc(s_power, 1)
                dve.wait_ge(s_power, 3 * n + 2)
                dve.reciprocal(scale, power).then_inc(s_power, 1)
                dve.wait_ge(s_power, 3 * n + 3)
                dve.tensor_scalar(scale, scale, WSCALE, None, ALU.mult).then_inc(s_wscale, 1)
                dve.tensor_scalar(unscale, power, 1 / (WSCALE * XSCALE), None, ALU.mult).then_inc(s_wscale, 1)

            def row_max(dst, src):
                dve.tensor_reduce(dst, src, AX.X, ALU.max, apply_absolute_value=True).then_inc(s_wmax, 1)

            def weight_scale(n):
                arrived(dve, n)
                row_max(w_max[:, n:n + 1], slots[n % SLOTS])
                dve.wait_ge(s_wmax, n + 1)
                split_scales(w_max[:, n:n + 1], w_pow[:, n:n + 1], w_scale[:, n:n + 1],
                             attn_unscale[:, n:n + 1], n)

            def ffn_max(j):
                arrived(dve, KB + j)
                row_max(f_max[:, j:j + 1], slots[(KB + j) % SLOTS])

            def weight_lo(n):
                rows, src, scale = rows_of(n)
                hi, lo = split_of(n)
                dve.wait_ge(s_wscale, 2 * min(n, KB) + 2)
                dve.wait_ge(s_whi, n + 1)
                dve.scalar_tensor_tensor(out=lo, in0=src, scalar=scale, in1=hi, op0=ALU.mult,
                                         op1=ALU.subtract).then_inc(s_wlo[0], 1)

            def copy_weight_lo(n):
                dve.wait_ge(s_wturn, 2 * n + 2)
                dve.tensor_copy(weights_of(n, 1), turned(n, 1)).then_inc(s_wcopy_lo, 1)

            dve.wait_ge(s_small, 80)
            link(dve.tensor_scalar, exp_in, exp_in, -87.0, 88.0, ALU.max, ALU.min)
            link(dve.tensor_scalar, exp_k, exp_in, 1 / LN2, MAGIC, ALU.mult, ALU.add)
            link(dve.tensor_scalar, exp_k, exp_k, MAGIC, None, ALU.subtract)
            link(dve.scalar_tensor_tensor, out=exp_in, in0=exp_k, scalar=-LN2_HI, in1=exp_in, op0=ALU.mult,
                                          op1=ALU.add)
            link(dve.scalar_tensor_tensor, out=exp_in, in0=exp_k, scalar=-LN2_LO, in1=exp_in, op0=ALU.mult,
                                          op1=ALU.add)
            link(dve.tensor_scalar, exp_out, exp_in, 1 / factorial(7), None, ALU.mult)
            for k in range(6, 0, -1):
                link(dve.scalar_tensor_tensor, out=exp_out, in0=exp_out, scalar=1 / factorial(k), in1=exp_in,
                                              op0=ALU.add, op1=ALU.mult)
            link(dve.tensor_scalar, exp_k.bitcast(U32), exp_k, 127.0, 2.0 ** 23, ALU.add, ALU.mult)
            link(dve.scalar_tensor_tensor, out=exp_out, in0=exp_out, scalar=1.0, in1=exp_k, op0=ALU.add,
                                          op1=ALU.mult)
            assert done[0] == EXPS
            for k in range(2):
                link(dve.tensor_scalar, zr[:, k, :], ea, dt, -1.0, ALU.mult, ALU.mult)
                link(dve.tensor_scalar, zi[:, k, :], ai, dt, None, ALU.mult)
            tt(ph, zi[:, 0:1, :].broadcast_to((P, NA, N)), steps_a[:, :].unsqueeze(2).broadcast_to((P, NA, N)),
               ALU.mult)
            tt(wexp, zr[:, 0:1, :].broadcast_to((P, KB, N)),
               steps_a[:, 2:NA].unsqueeze(2).broadcast_to((P, KB, N)), ALU.mult)
            weight_scale(0)
            dve.wait_ge(s_pre_act, 4)
            link(dve.tensor_scalar, kk, kk, MAGIC, None, ALU.subtract)
            link(dve.scalar_tensor_tensor, out=ph, in0=kk, scalar=-TWO_PI_HI, in1=ph, op0=ALU.mult, op1=ALU.add)
            link(dve.scalar_tensor_tensor, out=ph, in0=kk, scalar=-TWO_PI_LO, in1=ph, op0=ALU.mult, op1=ALU.add)
            link(dve.tensor_scalar, ph, ph, BELOW_PI, -BELOW_PI, ALU.min, ALU.max)
            link(dve.tensor_scalar, ph_abs.bitcast(U32), ph.bitcast(U32), NOT_SIGN, None, ALU.bitwise_and)
            weight_scale(1)
            weight_lo(0)
            dve.wait_ge(s_pre_act, 6)
            link(dve.scalar_tensor_tensor, out=em, in0=ex, scalar=1.0, in1=th, op0=ALU.add, op1=ALU.mult)
            link(dve.scalar_tensor_tensor, out=cm, in0=sn[:, 0, :], scalar=-2.0, in1=sn[:, 0, :], op0=ALU.mult,
                                          op1=ALU.mult)
            tt(e_re, em, cs[:, 1, :], ALU.mult)
            tt(e_re, e_re, cm, ALU.add)
            tt(e_im, ex, sn[:, 1, :], ALU.mult)
            tt(tmp, ea, ea, ALU.mult)
            tt(den, ai, ai, ALU.mult)
            tt(den, den, tmp, ALU.add)
            link(dve.reciprocal, den, den)
            tt(tmp, e_im, ai, ALU.mult)
            tt(t_re, e_re, ea, ALU.mult)
            tt(t_re, tmp, t_re, ALU.subtract)
            tt(t_re, t_re, den, ALU.mult)
            tt(tmp, e_re, ai, ALU.mult)
            tt(t_im, e_im, ea, ALU.mult)
            link(dve.scalar_tensor_tensor, out=t_im, in0=t_im, scalar=-1.0, in1=tmp, op0=ALU.mult,
                                          op1=ALU.subtract)
            tt(t_im, t_im, den, ALU.mult)
            b_re, b_im = bb[:, :, 0], bb[:, :, 1]
            tt(tmp, b_im, t_im, ALU.mult)
            tt(g_re, b_re, t_re, ALU.mult)
            tt(g_re, g_re, tmp, ALU.subtract)
            tt(tmp2, b_im, t_re, ALU.mult)
            tt(g_im, b_re, t_im, ALU.mult)
            tt(g_im, g_im, tmp2, ALU.add)
            assert done[0] == EXPS + 34
            dve.wait_ge(s_pre_dve, EXPS + 34)
            dve.tensor_tensor(w_re, wexp, cs[:, 2:NA, :], ALU.mult)
            link(dve.tensor_tensor, w_im, wexp, sn[:, 2:NA, :], ALU.mult)
            gr = g_re.unsqueeze(1).broadcast_to((P, KB, N))
            gi = g_im.unsqueeze(1).broadcast_to((P, KB, N))
            dve.wait_ge(s_pre_dve, EXPS + 35)
            dve.tensor_tensor(qa, w_re, gr, ALU.mult)
            link(dve.tensor_tensor, qb, w_im, gi, ALU.mult)
            tt(q1n[:, :, 0:N], qa, qb, ALU.subtract)
            dve.wait_ge(s_pre_dve, EXPS + 37)
            dve.tensor_tensor(qa, w_im, gr, ALU.mult)
            link(dve.tensor_tensor, qb, w_re, gi, ALU.mult)
            link(dve.scalar_tensor_tensor, out=q1n[:, :, N:2 * N], in0=qa, scalar=-1.0, in1=qb, op0=ALU.mult,
                                          op1=ALU.subtract)
            dve.wait_ge(s_pre_dve, EXPS + 39)
            dve.tensor_scalar(q2n[:, :, 0:N], q1n[:, :, N:2 * N], 2.0, None, ALU.mult)
            link(dve.tensor_scalar, q2n[:, :, N:2 * N], q1n[:, :, 0:N], -2.0, None, ALU.mult)
            link(dve.tensor_scalar, q1n, q1n, 2.0, None, ALU.mult)
            assert done[0] == EXPS + 41

            def reduce_phase(T):
                dve.wait_ge(s_turns, T + 1)
                k, r = turn[:, :, :], phase[:, :, :]
                dve.tensor_scalar(k, k, MAGIC, None, ALU.subtract).then_inc(s_reduce, 1)
                dve.wait_ge(s_reduce, 5 * T + 1)
                dve.scalar_tensor_tensor(out=r, in0=k, scalar=-TWO_PI_HI, in1=r, op0=ALU.mult, op1=ALU.add)\
                    .then_inc(s_reduce, 1)
                dve.wait_ge(s_reduce, 5 * T + 2)
                dve.scalar_tensor_tensor(out=r, in0=k, scalar=-TWO_PI_LO, in1=r, op0=ALU.mult, op1=ALU.add)\
                    .then_inc(s_reduce, 1)
                dve.wait_ge(s_reduce, 5 * T + 3)
                dve.tensor_scalar(phase[0:N, :, :].bitcast(U32), phase[0:N, :, :].bitcast(U32), NOT_SIGN, None,
                                  ALU.bitwise_and).then_inc(s_reduce, 1)
                dve.tensor_scalar(phase[N:P, :, :], phase[N:P, :, :], BELOW_PI, -BELOW_PI, ALU.min, ALU.max)\
                    .then_inc(s_reduce, 1)

            def make_u(T):
                dve.wait_ge(s_sin, T + 1)
                dve.wait_ge(s_decay, T + 1)
                at_least(dve, s_s4, 4 * T)
                dve.tensor_tensor(u[:, :, :], decay[:, :, :], turn[:, :, :], ALU.mult).then_inc(s_u, 1)

            def make_m(T):
                dve.wait_ge(s_terms, 2 * T + 2)
                dve.tensor_tensor(m[:, :, :, :], m[:, :, :, :], m_im[:, :, :, :], ALU.add).then_inc(s_m, 1)

            def block_sum(dst, src):
                return dve.tensor_reduce(dst[:, :], src[:, :, :].rearrange("p k t -> p t k"), AX.X, ALU.add)

            def sum1(T):
                dve.wait_ge(s_h, 4 * T + 4)
                at_least(dve, s_mean1, T)
                block_sum(sum_1, h).then_inc(s_sum1, 1)

            def centre1(T):
                dve.wait_ge(s_mean1, T + 1)
                at_least(dve, s_x1, T)
                dve.tensor_tensor(d1[:, :, :], h[:, :, :],
                                  ps_stat[:, 0:TT].unsqueeze(1).broadcast_to((P, KB, TT)), ALU.subtract)\
                    .then_inc(s_d1, 1)

            def square_sum(T, ssq, ready, product, s):
                dve.wait_ge(ready, T + 1)
                at_least(dve, product, T)
                block_sum(ssq, squares).then_inc(s, 1)

            def variance(T, var, product, normalised, s):
                dve.wait_ge(product, T + 1)
                at_least(dve, normalised, T)
                dve.tensor_scalar(var[:, :], ps_stat[:, 0:TT], EPS, None, ALU.add).then_inc(s, 1)

            def normalise(T, d, var, rstd, guess, step_done, s):
                dve.wait_ge(guess, T + 1)
                dve.tensor_tensor(newton[:, :], rstd[:, :], rstd[:, :], ALU.mult).then_inc(step_done, 1)
                dve.wait_ge(step_done, 4 * T + 1)
                dve.tensor_tensor(newton[:, :], newton[:, :], var[:, :], ALU.mult).then_inc(step_done, 1)
                dve.wait_ge(step_done, 4 * T + 2)
                dve.tensor_scalar(newton[:, :], newton[:, :], -0.5 * XSCALE, 1.5 * XSCALE, ALU.mult, ALU.add)\
                    .then_inc(step_done, 1)
                dve.wait_ge(step_done, 4 * T + 3)
                dve.tensor_tensor(rstd[:, :], rstd[:, :], newton[:, :], ALU.mult).then_inc(step_done, 1)
                dve.wait_ge(step_done, 4 * T + 4)
                dve.tensor_tensor(d[:, :, :], d[:, :, :], rstd[:, :].unsqueeze(1).broadcast_to((P, KB, TT)),
                                  ALU.mult).then_inc(s, 1)

            def low_part(T, d, hi, lo, ready, s):
                dve.wait_ge(ready, T + 1)
                dve.tensor_tensor(lo[:, :, :], d[:, :, :], hi[:, :, :], ALU.subtract).then_inc(s, 1)

            def norm1_end(T):
                normalise(T, d1, var_1, rstd_1, s_y1, s_nw1, s_xn1)
                low_part(T, d1, x1_hi, x1_lo, s_hi1, s_x1)

            def add_h(t, j2):
                dve.wait_ge(s_attn_sb, 4 * t + j2 + 1)
                if j2 == 0:
                    at_least(dve, s_h2t, 2 * t)
                    at_least(dve, s_d2, t)
                ks = slice(2 * j2, 2 * j2 + 2)
                dve.tensor_tensor(h2[:, ks, :], attn_out[:, j2 % 2, :, :], h[:, ks, :], ALU.add).then_inc(s_h2, 1)

            def sum2(t):
                dve.wait_ge(s_h2, 4 * t + 4)
                at_least(dve, s_mean2, t)
                block_sum(sum_2, h2).then_inc(s_sum2, 1)

            def gate(t):
                p = ps_gate[:, 0:SUB * G].rearrange("p (s g) -> p s g", g=G)
                k = 9 * t
                dve.wait_ge(s_proj, t + 1)
                dve.tensor_reduce(gate_stat[:, :], p[:, :, ER:G], AX.X, ALU.max).then_inc(s_soft, 1)
                dve.wait_ge(s_soft, k + 1)
                dve.tensor_tensor(gates[:, :, :], p[:, :, ER:G],
                                  gate_stat[:, :].unsqueeze(2).broadcast_to((P, SUB, E)), ALU.subtract)\
                    .then_inc(s_soft, 1)
                dve.wait_ge(s_gexp, t + 1)
                dve.tensor_reduce(gate_stat[:, :], gates[:, :, :], AX.X, ALU.add).then_inc(s_soft, 1)
                dve.wait_ge(s_soft, k + 3)
                dve.reciprocal(gate_stat[:, :], gate_stat[:, :]).then_inc(s_soft, 1)
                dve.wait_ge(s_soft, k + 4)
                dve.tensor_tensor(gates[:, :, :], gates[:, :, :],
                                  gate_stat[:, :].unsqueeze(2).broadcast_to((P, SUB, E)), ALU.mult)\
                    .then_inc(s_soft, 1)
                dve.wait_ge(s_soft, k + 5)
                dve.tensor_tensor(lora[:, :, :].rearrange("p s (e r) -> p s e r", e=E),
                                  p[:, :, 0:ER].rearrange("p s (e r) -> p s e r", e=E),
                                  gates[:, :, :].unsqueeze(3).broadcast_to((P, SUB, E, R)), ALU.mult)\
                    .then_inc(s_soft, 1)
                dve.wait_ge(s_soft, k + 6)
                at_least(dve, s_lora_t, t)
                dve.tensor_copy(lora_split[:, :, 0:ER], lora[:, :, :]).then_inc(s_soft, 1)
                dve.tensor_copy(lora_split[:, :, ER:2 * ER], lora[:, :, :]).then_inc(s_soft, 1)
                dve.wait_ge(s_soft, k + 7)
                dve.tensor_tensor(lora_split[:, :, 2 * ER:3 * ER], lora[:, :, :],
                                  lora_split[:, :, 0:ER].bitcast(F32), ALU.subtract).then_inc(s_soft, 1)

            def copy_lora(t):
                dve.wait_ge(s_lora_t, t + 1)
                at_least(dve, s_ffn, 2 * t)
                dve.tensor_copy(lora_t[:, :, :].rearrange("p a b -> p (a b)"), ps_gate[0:KL, P:P + SUB * P])\
                    .then_inc(s_lora_sb, 1)

            def finish(t, i):
                dve.wait_ge(s_ffn, 2 * t + i + 1)
                dve.wait_ge(s_h2_tok, 2 * t + i + 1)
                at_least(dve, s_out[i], 16 * t)
                if isinstance(t, int) and t == TILES - 1:
                    for o in range(2):
                        cols = slice(o * HALF, (o + 1) * HALF)
                        ins = dve.scalar_tensor_tensor(out=result[:, i, cols], in0=acc_of(t, i)[o],
                                                       scalar=ffn_unscale[:, :], in1=h2_tok[:, i, cols],
                                                       op0=ALU.mult, op1=ALU.add)
                    ins.then_inc(s_result, 1)
                    return
                dve.scalar_tensor_tensor(out=result[:, i, :], in0=ps_ffn[i][:, :, :].rearrange("p a b -> p (a b)"),
                                         scalar=ffn_unscale[:, :], in1=h2_tok[:, i, :], op0=ALU.mult,
                                         op1=ALU.add).then_inc(s_result, 1)

            reduce_phase(0)
            weight_scale(2)
            dve.wait_ge(s_xt_sb, 1)
            dve.wait_ge(s_pre_act, 8)
            c, f, dst = m_term(0, 0)
            dve.tensor_tensor(dst, c, f, ALU.mult).then_inc(s_terms, 1)
            make_u(0)
            weight_scale(3)
            make_m(0)
            weight_lo(2)
            weight_scale(4)
            weight_scale(5)
            sum1(0)
            weight_lo(4)
            centre1(0)
            weight_scale(6)
            square_sum(0, ssq_1, s_sq1, s_var1, s_ssq1)
            weight_scale(7)
            variance(0, var_1, s_var1, s_xn1, s_vv1)
            weight_lo(6)
            normalise(0, d1, var_1, rstd_1, s_y1, s_nw1, s_xn1)
            dve.wait_ge(s_wg, 32)
            row_max(f_max[0:G, KB:KB + 1], wg_rows)
            ffn_max(0)
            low_part(0, d1, x1_hi, x1_lo, s_hi1, s_x1)
            for j in range(1, KB - 2):
                ffn_max(j)
            ffn_max(6)
            ffn_max(7)
            dve.wait_ge(s_wmax, 2 * KB + 1)
            dve.tensor_reduce(f_top[:, 0:1], f_max[:, :], AX.X, ALU.max).then_inc(s_wmax, 1)
            dve.wait_ge(s_lb, 16 * (KB + 1))
            dve.tensor_scalar(lbm, lbm, LORA_SCALE, None, ALU.mult).then_inc(s_lbn, 1)
            dve.wait_ge(s_lbn, 1)
            dve.tensor_copy(lbn[:, :, 0:ER], lbm)
            dve.tensor_copy(lbn[:, :, 2 * ER:3 * ER], lbm)
            dve.tensor_copy(lbn[:, :, KL - 2:KL - 1], lbb.unsqueeze(2)).then_inc(s_lbn, 1)
            dve.wait_ge(s_lbn, 2)
            dve.tensor_tensor(lbn[:, :, ER:2 * ER], lbm, lbn[:, :, 0:ER].bitcast(F32), ALU.subtract)
            dve.tensor_tensor(lbn[:, :, KL - 1:KL], lbb.unsqueeze(2), lbn[:, :, KL - 2:KL - 1].bitcast(F32),
                              ALU.subtract).then_inc(s_lbn, 1)
            dve.wait_ge(s_wall, 2)
            split_scales(f_top[:, 1:2], f_pow[:, :], ffn_scale[:, :], ffn_unscale[:, :], KB)
            dve.wait_ge(s_wscale, 2 * KB + 2)
            dve.tensor_scalar(lora_split[:, :, KL - 2:KL],
                              mean_w[:, 0:2 * SUB].rearrange("p (a b) -> p a b", a=SUB), ffn_scale[:, :],
                              L * XSCALE, ALU.mult, ALU.mult).then_inc(s_lbn, 1)

            weight_lo(8)
            add_h(0, 0)
            weight_lo(9)
            add_h(0, 1)
            reduce_phase(1)
            copy_weight_lo(8)
            weight_lo(10)
            copy_weight_lo(9)
            weight_lo(11)
            make_u(1)
            make_m(1)
            add_h(0, 2)
            copy_weight_lo(10)
            weight_lo(12)
            copy_weight_lo(11)
            add_h(0, 3)
            weight_lo(13)
            sum2(0)
            sum1(1)
            copy_weight_lo(12)
            weight_lo(14)
            centre1(1)
            copy_weight_lo(13)
            square_sum(1, ssq_1, s_sq1, s_var1, s_ssq1)
            weight_lo(15)
            copy_weight_lo(14)
            variance(1, var_1, s_var1, s_xn1, s_vv1)
            weight_lo(16)
            copy_weight_lo(15)
            norm1_end(1)
            copy_weight_lo(16)

            def step(t):
                square_sum(t - 1, ssq_2, s_sq2, s_var2, s_ssq2)
                reduce_phase(t + 1)
                add_h(t, 0)
                make_u(t + 1)
                variance(t - 1, var_2, s_var2, s_xn2, s_vv2)
                add_h(t, 1)
                normalise(t - 1, d2, var_2, rstd_2, s_y2, s_nw2, s_xn2)
                add_h(t, 2)
                make_m(t + 1)
                low_part(t - 1, d2, x2_hi, x2_lo, s_hi2, s_x2)
                add_h(t, 3)
                sum2(t)
                sum1(t + 1)
                gate(t - 1)
                centre1(t + 1)
                square_sum(t + 1, ssq_1, s_sq1, s_var1, s_ssq1)
                copy_lora(t - 1)
                finish(t - 1, 0)
                variance(t + 1, var_1, s_var1, s_xn1, s_vv1)
                norm1_end(t + 1)
                finish(t - 1, 1)

            step(1)
            with dve.Fori(2, TILES - 1) as t:
                step(t)
            t = TILES - 1
            square_sum(t - 1, ssq_2, s_sq2, s_var2, s_ssq2)
            add_h(t, 0)
            variance(t - 1, var_2, s_var2, s_xn2, s_vv2)
            add_h(t, 1)
            normalise(t - 1, d2, var_2, rstd_2, s_y2, s_nw2, s_xn2)
            add_h(t, 2)
            low_part(t - 1, d2, x2_hi, x2_lo, s_hi2, s_x2)
            add_h(t, 3)
            sum2(t)
            gate(t - 1)
            copy_lora(t - 1)
            finish(t - 1, 0)
            square_sum(t, ssq_2, s_sq2, s_var2, s_ssq2)
            variance(t, var_2, s_var2, s_xn2, s_vv2)
            normalise(t, d2, var_2, rstd_2, s_y2, s_nw2, s_xn2)
            finish(t - 1, 1)
            low_part(t, d2, *x2_of(t), s_hi2, s_x2)
            gate(t)
            copy_lora(t)
            finish(t, 0)
            finish(t, 1)


_INS = ["x", "L0_tok_log_dt", "L0_tok_B", "L0_tok_inv_A_real", "L0_tok_A_imag", "L0_attn_weight",
        "L0_attn_bias", "L0_ffn_W", "L0_ffn_b", "L0_ffn_A", "L0_ffn_Bm", "L0_ffn_Wr"]


def kernel(**inputs):
    import numpy as np
    import concourse.bacc as bacc
    from concourse.bass_utils import run_bass_kernel_spmd

    nc = bacc.Bacc("TRN2", target_bir_lowering=False, num_devices=1)
    arrays, args = {}, []
    for name in _INS:
        a = np.ascontiguousarray(inputs[name])
        arrays[f"in_{name}"] = a
        args.append(nc.dram_tensor(f"in_{name}", a.shape, mybir.dt.from_np(a.dtype), kind="ExternalInput").ap())
    args.append(nc.dram_tensor("out", (C, H, L), F32, kind="ExternalOutput").ap())
    program(nc, *args)
    result = run_bass_kernel_spmd(nc, [arrays], core_ids=[0])
    return result.results[0]["out"]
```
